# Optimizing a Trainium2 kernel written in Bass

```python
import numpy as np
import jax
import jax.numpy as jnp

def _softmax(x, axis=-1):
    return jax.nn.softmax(x, axis=axis)
def _gelu(x):
    return jax.nn.gelu(x, approximate=True)
def _silu(x):
    return jax.nn.silu(x)
def _sigmoid(x):
    return jax.nn.sigmoid(x)
def _layernorm(x, axis=-1, eps=1e-5):
    m = jnp.mean(x, axis=axis, keepdims=True)
    v = jnp.var(x, axis=axis, keepdims=True)
    return (x - m) / jnp.sqrt(v + eps)
def _scatter_add(tgt, idx, src, axis=0):
    return tgt.at[idx].add(src)
def _segment_sum(src, seg, n):
    return jax.ops.segment_sum(src, seg, n)

kernel_name = 'mk_adj_ffn_d1_adj_256_2352ec'

def setup_inputs(seed: int = 0):
    np.random.seed(seed)
    _w = jnp.asarray
    def _rec_inputs():
        import jax
        import jax.numpy as jnp
        _gk = jax.random.key(seed)
        x = -0.0005207 + 1.001 * jax.random.normal(jax.random.fold_in(_gk, 1), (64, 256, 256), jnp.float32)
        _a = jax.random.bernoulli(jax.random.fold_in(_gk, 2), 0.015625, (256, 256))
        adj = _a.astype(jnp.int32)
        return x, adj
    x, adj = _rec_inputs()
    def _L0_gnn_setup():
        import jax, jax.numpy as jnp
        import numpy as np
        B, N, IN_F = (8, 1024, 256)
        N_H, D_F = (4, 64)
        NEG_SLOPE = 0.2
        key = jax.random.key(seed)
        k1, k2, k3, k4 = jax.random.split(key, 4)
        h = jax.random.normal(k1, (B, N, IN_F), dtype=jnp.float32)
        adj = jax.random.randint(k2, (N, N), 0, 2, dtype=jnp.int32)
        W = jax.random.normal(k3, (IN_F, N_H * D_F), dtype=jnp.float32) * IN_F ** (-0.5)
        a = jax.random.normal(k4, (N_H, 2 * D_F), dtype=jnp.float32) * D_F ** (-0.5)
        return {'h': h, 'adj': adj, 'W': W, 'a': a}
    _L0_gnn_all = _L0_gnn_setup()
    _L0_gnn_in = {k: v for k, v in _L0_gnn_all.items() if k in ('W', 'a', )}
    del _L0_gnn_all

    def _L0_ffn_setup():
        import jax, jax.numpy as jnp
        import numpy as np
        C = 256
        EPS = 1e-05
        N_ITERS = 30

        def _layernorm(x, w, bias):
            mu = jnp.mean(x, axis=-1, keepdims=True)
            var = jnp.mean(jnp.square(x - mu), axis=-1, keepdims=True)
            return (x - mu) * jax.lax.rsqrt(var + EPS) * w + bias
        key = jax.random.key(seed)
        kx, kw, kb, klw, klb = jax.random.split(key, 5)
        x = jax.random.normal(kx, (8, 2048, C), dtype=jnp.float32)
        bound = 1.0 / np.sqrt(C)
        W = jax.random.uniform(kw, (C, C), minval=-bound, maxval=bound, dtype=jnp.float32)
        b = jax.random.uniform(kb, (C,), minval=-bound, maxval=bound, dtype=jnp.float32)
        ln_w = jnp.ones((C,), dtype=jnp.float32)
        ln_b = jnp.zeros((C,), dtype=jnp.float32)
        return {'x': x, 'ln_w': ln_w, 'ln_b': ln_b, 'W': W, 'b': b}
    _L0_ffn_all = _L0_ffn_setup()
    _L0_ffn_in = {k: v for k, v in _L0_ffn_all.items() if k in ('ln_w', 'ln_b', 'W', 'b', )}
    del _L0_ffn_all

    return {
        "x": x,
        "adj": adj,
        "L0_gnn_W": _L0_gnn_in["W"],
        "L0_gnn_a": _L0_gnn_in["a"],
        "L0_ffn_ln_w": _L0_ffn_in["ln_w"],
        "L0_ffn_ln_b": _L0_ffn_in["ln_b"],
        "L0_ffn_W": _L0_ffn_in["W"],
        "L0_ffn_b": _L0_ffn_in["b"],
    }

def reference(x, adj, L0_gnn_W, L0_gnn_a, L0_ffn_ln_w, L0_ffn_ln_b, L0_ffn_W, L0_ffn_b):
    import jax
    import jax.numpy as jnp
    def _L0_gnn_ref(h, adj, W, a):
        import jax, jax.numpy as jnp
        import numpy as np
        B, N, IN_F = (8, 1024, 256)
        N_H, D_F = (4, 64)
        NEG_SLOPE = 0.2
        Wh = (h @ W).reshape(h.shape[0], h.shape[1], N_H, D_F)
        a_src, a_dst = (a[:, :D_F], a[:, D_F:])
        s_src = jnp.einsum('bnhd,hd->bnh', Wh, a_src)
        s_dst = jnp.einsum('bnhd,hd->bnh', Wh, a_dst)
        e = s_src[:, :, None, :] + s_dst[:, None, :, :]
        e = jnp.where(e > 0, e, NEG_SLOPE * e)
        mask = (adj != 0)[None, :, :, None]
        e = jnp.where(mask, e, -jnp.inf)
        alpha = jax.nn.softmax(e, axis=2)
        alpha = jnp.nan_to_num(alpha, nan=0.0)
        h_out = jnp.einsum('bijh,bjhd->bihd', alpha, Wh)
        h_out = h_out.reshape(h.shape[0], h.shape[1], N_H * D_F)
        return jax.nn.elu(h_out)

    def _L0_ffn_ref(x, ln_w, ln_b, W, b):
        import jax, jax.numpy as jnp
        import numpy as np
        C = 256
        EPS = 1e-05
        N_ITERS = 30

        def _layernorm(x, w, bias):
            mu = jnp.mean(x, axis=-1, keepdims=True)
            var = jnp.mean(jnp.square(x - mu), axis=-1, keepdims=True)
            return (x - mu) * jax.lax.rsqrt(var + EPS) * w + bias
        def step(h, _):
            h = h + 0.01 * jnp.tanh(h)
            h = h * jax.nn.sigmoid(h)
            h = _layernorm(h, ln_w, ln_b)
            h = jnp.einsum('bsc,dc->bsd', h, W) + b
            return (h, None)
        x, _ = jax.lax.scan(step, x, None, length=N_ITERS)
        return x

    x = x + _L0_gnn_ref(_layernorm(x, axis=-1), adj, L0_gnn_W, L0_gnn_a)
    x = x + _L0_ffn_ref(_layernorm(x, axis=-1), L0_ffn_ln_w, L0_ffn_ln_b, L0_ffn_W, L0_ffn_b)
    return x


_drawn_inputs = setup_inputs


def setup_inputs(seed=0):
    import zlib

    import numpy as np

    out = dict(_drawn_inputs(seed))
    spreads = {'L0_ffn_ln_w': (1.0, 0.2), 'L0_ffn_ln_b': (0.0, 0.1)}
    factors = {}
    for name, (base, spread) in spreads.items():
        noise = np.random.default_rng([zlib.crc32(name.encode()), seed]).standard_normal(out[name].shape)
        drawn = base * np.exp(spread * noise) if base else spread * noise
        out[name] = jnp.asarray(drawn.astype(out[name].dtype))
    for name, factor in factors.items():
        out[name] = (out[name] * factor).astype(out[name].dtype)
    return out
```

```python
import concourse.bass as bass
import concourse.mybir as mybir
from contextlib import ExitStack
import numpy as np

F32 = mybir.dt.float32
F32R = mybir.dt.float32r
I32 = mybir.dt.int32
ALU = mybir.AluOpType
ACT = mybir.ActivationFunctionType
AX = mybir.AxisListType

P = 128
B, N, C = 64, 256, 256
HEADS, DH = 4, 64
NB = N // P
CB = C // P
EPS = 1e-5
SLOPE = 0.2
STEPS = 30
GAIN = 100.0
MASKED = -1e30

GBODY = 4
HBODY = NB * GBODY
HALVES = NB * B
SD = 2 * HEADS

UT = 4
UNITS = 8
UF = UT * C
ROWS = B * N
BATCHES = ROWS // (P * UT * UNITS)
SLOTS = STEPS * UNITS
NORMS = SLOTS + UNITS


SETUP_STEPS = 3 + 3 + 4 * CB + 4


def freed(eng, sem, count):
    if not (isinstance(count, int) and count <= 0):
        eng.wait_ge(sem, count)


def scan_slots(eng, total, body, lags, slot, peeled=1):
    low, high = min(lags), max(lags)
    assert high <= body
    stop = (total + low) // body if low < 0 else total // body
    for s in range(low, peeled * body):
        k = max(s, 0) // body
        slot(k, s - k * body, lambda l, s=s: 0 <= s - l < total)
    with eng.Fori(peeled, stop) as k:
        for j in range(body):
            slot(k, j, lambda l: True)
    for s in range(stop * body, total + high):
        slot(stop, s - stop * body, lambda l, s=s: 0 <= s - l < total)


def build(nc, x, adj, gnn_w, gnn_a, ln_w, ln_b, ffn_w, ffn_b, x1, out):
    ctx = ExitStack()
    with ctx:
        def sb(name, shape, dt=F32):
            return ctx.enter_context(nc.sbuf_tensor(name, shape, dt))

        def sem(name):
            return ctx.enter_context(nc.semaphore(name))

        ident = sb("ident", [P, P])
        avg = sb("avg", [P, P])
        exponent = sb("exponent", [P, 8])
        eps_t = sb("eps_t", [P, 8])
        gain_t = sb("gain_t", [P, 8])
        gw = sb("gw", [P, CB, C + SD])
        a_bc = sb("a_bc", [P, HEADS, 2, DH])
        prod = sb("prod", [P, HEADS, DH])
        adj_i = sb("adj_i", [P, NB, N], I32)
        mask = sb("mask", [P, NB, N])
        edge = sb("edge", [P, NB, N])
        has_edge = sb("has_edge", [P, NB])
        head_rows = sb("head_rows", [16, HEADS])
        w_raw = sb("w_raw", [P, CB, C])
        w_t = sb("w_t", [P, CB, C])
        w_s = sb("w_s", [P, CB, C])
        w_c = sb("w_c", [P, CB, C])
        lnw = sb("lnw", [P, CB])
        lnb = sb("lnb", [P, CB])
        lnb_wide = sb("lnb_wide", [P, CB, P])
        b_bc = sb("b_bc", [P, C])
        c_sum = sb("c_sum", [P, C])
        c_bc = sb("c_bc", [P, C])
        xin = sb("xin", [P, 2, NB, C])
        xres = sb("xres", [P, 2, NB, C])
        g_st = sb("g_st", [P, 2, NB, 6])
        g_mv = sb("g_mv", [P, 2, NB, 2])
        g_ve = sb("g_ve", [P, 2, NB])
        g_rstd = sb("g_rstd", [P, 2, NB])
        hn = sb("hn", [P, 2, NB, C])
        hnt = sb("hnt", [P, 2, CB, N])
        wh = sb("wh", [P, GBODY, NB, C])
        sd = sb("sd", [P, NB, 8, 4])
        lr = sb("lr", [16, 2, 2, N], F32R)
        rh = sb("rh", [16, 2, HEADS, N], F32R)
        em = sb("em", [P, 2, HEADS, N])
        mx = sb("mx", [P, 2, HEADS])
        mxl = sb("mxl", [P, 2, HEADS])
        nmx = sb("nmx", [P, 2, HEADS])
        rs = sb("rs", [P, 4, HEADS])
        rcp = sb("rcp", [P, 2, HEADS])
        rnorm = sb("rnorm", [P, 4, HEADS])
        ets = sb("ets", [P, 2, HEADS, NB, P])
        att = sb("att", [P, GBODY, NB, C])
        neg = sb("neg", [P, 2, NB, C])
        x1_sb = sb("x1_sb", [P, UNITS, UF])
        st = sb("st", [P, UNITS, UT, 6])
        mv = sb("mv", [P, UNITS, UT, 2])
        ve = sb("ve", [P, UNITS, UT])
        rstd = sb("rstd", [P, UNITS, UT])
        rstd_g = sb("rstd_g", [P, UNITS, UT])
        state = sb("state", [P, UNITS, UF])
        TR = 4
        th = sb("th", [P, TR, UF])
        GR = 4
        gts = sb("gts", [P, GR, CB, UT * P])
        ps = ctx.enter_context(nc.psum_tensor("ps", [P, 8, 512], F32))

        ps_t = ps[:, 0, :]
        ps_wh = ps[:, 1:3, 0:C + SD]
        ps_e = ps[:, 3:5, :]
        ps_o = ps[:, 5, :]
        ps_et = ps[:, 6:8, :]

        s_in = sem("weights_loaded")
        s_id = sem("ident_ready")
        s_set = sem("setup_dve")
        s_wt = sem("w_transposed")
        s_cm = sem("colmean_ready")
        s_cv = sem("c_ready")
        s_xin = [sem(f"xin_loaded{r}") for r in range(2)]
        s_xres = [sem(f"xres_loaded{r}") for r in range(2)]
        s_x1st = [sem(f"x1_stored{r}") for r in range(2)]
        s_gbn = sem("g_bn")
        s_gmv = sem("g_meanvar")
        s_gve = sem("g_ve")
        s_grs = sem("g_rstd")
        s_hn = sem("hn_ready")
        s_hnp = sem("hn_transposed")
        s_hnt = sem("hnt_copied")
        s_wh = sem("wh_done")
        s_whc = sem("wh_copied")
        s_sdh = sem("sd_hi")
        s_sdl = sem("sd_lo")
        s_lrp = sem("lr_transposed")
        s_lr = sem("lr_copied")
        s_rh = sem("rh_ready")
        s_e = sem("scores_ready")
        s_ttr = sem("scores_masked")
        s_mxl = sem("max_lrelu")
        s_nmx = sem("neg_max")
        s_l = sem("lrelu_done")
        s_exp = sem("exp_done")
        s_te = sem("probs_transposed")
        s_et = sem("probs_copied")
        s_o = sem("attended")
        s_rcp = sem("rcp_ready")
        s_rn = sem("rnorm_ready")
        s_att = sem("att_ready")
        s_neg = sem("neg_ready")
        s_ex = sem("elu_exp")
        s_el = sem("elu_sum")
        s_x1 = sem("x1_ready")
        f_ld = [sem(f"f_loaded{u}") for u in range(UNITS)]
        f_st = [sem(f"f_stored{u}") for u in range(UNITS)]
        f_bn = sem("f_bn")
        f_mv = sem("f_meanvar")
        f_ve = sem("f_ve")
        f_rs = sem("f_rstd")
        f_rg = sem("f_rstd_gain")
        f_z = sem("state_ready")
        f_t = sem("tanh_done")
        f_u = sem("sum_done")
        f_g = sem("silu_done")
        f_tp = sem("g_transposed")
        f_tc = sem("gt_copied")
        f_mm = sem("product_done")
        f_out = sem("out_ready")
        passed = {e: sem(f"passed_{e}") for e in ("sp", "dve")}

        block = ctx.enter_context(nc.Block())

        def graph(t, k, j):
            g = k * GBODY + j
            return t.rearrange("(g i p) c -> g p i c", i=NB, p=P)[g]

        def unit(t, b, u):
            return t.rearrange("(b u p t) c -> b u p (t c)", u=UNITS, p=P, t=UT)[b, u]

        @block.sync
        def _(sp):
            sp.dma_start(gw[:, :, 0:C], gnn_w.rearrange("(k p) c -> p k c", p=P)).then_inc(s_in, 16)
            sp.dma_start(a_bc[:], gnn_a.rearrange("h (two d) -> h two d", two=2).unsqueeze(0)
                         .to_broadcast([P, HEADS, 2, DH])).then_inc(s_in, 16)
            sp.dma_start(adj_i[:], adj.rearrange("(i p) j -> p i j", p=P)).then_inc(s_in, 16)
            sp.dma_start(w_raw[:], ffn_w.rearrange("(k p) c -> p k c", p=P)).then_inc(s_in, 16)
            sp.dma_start(b_bc[:], ffn_b.unsqueeze(0).to_broadcast([P, C])).then_inc(s_in, 16)
            sp.dma_start(lnw[:], ln_w.rearrange("(k p) -> p k", p=P),
                         allow_slow_non_contiguous=True).then_inc(s_in, 16)
            sp.dma_start(lnb[:], ln_b.rearrange("(k p) -> p k", p=P),
                         allow_slow_non_contiguous=True).then_inc(s_in, 16)

            def slot(k, j, live):
                if live(-6):
                    g, r = j + 6, j % 2
                    freed(sp, s_hn, k * GBODY + g - 1)
                    sp.sem_inc(passed["sp"], 1)
                    sp.dma_start(xin[:, r], graph(x, k, g)).then_inc(s_xin[r], 16)
                if live(0):
                    g, r = j, j % 2
                    freed(sp, s_x1st[r], 16 * (2 * k + g // 2))
                    sp.sem_inc(passed["sp"], 1)
                    sp.dma_start(xres[:, r], graph(x, k, g)).then_inc(s_xres[r], 16)
                if live(1):
                    g, r = j - 1, (j - 1) % 2
                    sp.wait_ge(s_x1, k * GBODY + g + 1)
                    sp.sem_inc(passed["sp"], 1)
                    sp.dma_start(graph(x1, k, g), xres[:, r]).then_inc(s_x1st[r], 16)

            scan_slots(sp, B, GBODY, (-6, 0, 1), slot, peeled=2)
            for r in range(2):
                sp.wait_ge(s_x1st[r], 16 * (B // 2))
            with sp.Fori(0, BATCHES) as b:
                for u in range(UNITS):
                    sp.dma_start(x1_sb[:, u], unit(x1, b, u)).then_inc(f_ld[u], 16)
                for u in range(UNITS):
                    sp.wait_ge(f_out, b * UNITS + u + 1)
                    sp.sem_inc(passed["sp"], 1)
                    sp.dma_start(unit(out, b, u), x1_sb[:, u]).then_inc(f_st[u], 16)
                for u in range(UNITS):
                    sp.wait_ge(f_st[u], b * 16 + 16)
                    sp.sem_inc(passed["sp"], 1)

        @block.gpsimd
        def _(pool):
            nc.gpsimd.memset(ident[:], 0.0).then_inc(s_id, 1)
            nc.gpsimd.memset(head_rows[:], 0.0).then_inc(s_id, 1)
            pool.wait_ge(s_id, 2)
            nc.gpsimd.affine_select(out=ident[:], in_=ident[:], compare_op=ALU.not_equal, fill=1.0, base=0,
                                    pattern=[[-1, P]], channel_multiplier=1).then_inc(s_id, 1)
            for q in range(4):
                pool.wait_ge(s_id, 3 + q)
                nc.gpsimd.affine_select(out=head_rows[:], in_=head_rows[:], compare_op=ALU.not_equal,
                                        fill=1.0, base=-HEADS * q, pattern=[[-1, HEADS]],
                                        channel_multiplier=1).then_inc(s_id, 1)
            nc.gpsimd.memset(exponent[:], -0.5).then_inc(s_id, 1)
            nc.gpsimd.memset(eps_t[:], EPS).then_inc(s_id, 1)
            nc.gpsimd.memset(gain_t[:], GAIN).then_inc(s_id, 1)
            nc.gpsimd.memset(avg[:], 1.0 / C).then_inc(s_id, 1)
            pool.wait_ge(s_id, 11)

            def slot(k, j, live):
                if live(-6) and j % 2 == 0:
                    g = (j + 6) // 2
                    r = g % 2
                    pool.wait_ge(s_gmv, k * GBODY + g + 1)
                    nc.gpsimd.tensor_tensor(g_ve[:, r], g_mv[:, r, :, 1], eps_t[:, 0:NB],
                                            ALU.add).then_inc(s_gve, 1)
                    pool.wait_ge(s_gve, k * GBODY + g + 1)
                    nc.gpsimd.tensor_tensor(g_rstd[:, r], g_ve[:, r], exponent[:, 0:NB],
                                            ALU.pow).then_inc(s_grs, 1)
                if live(-1) and j % 2 == 1:
                    g = (j + 1) // 2
                    r = g % 2
                    pool.wait_ge(s_lr, k * GBODY + g + 1)
                    freed(pool, s_e, k * HBODY + 2 * g - 2)
                    for h in range(HEADS):
                        last = nc.gpsimd.tensor_tensor(rh[:, r, h], lr[:, r, 1].bitcast(F32),
                                                       head_rows[:, h:h + 1].to_broadcast([16, N]), ALU.mult)
                    last.then_inc(s_rh, 1)

            scan_slots(pool, HALVES, HBODY, (-6, -1), slot, peeled=2)

            with pool.Fori(0, BATCHES) as b:
                n0 = b * NORMS
                s0 = b * SLOTS

                def power(n, u):
                    pool.wait_ge(f_mv, n + 1)
                    nc.gpsimd.tensor_tensor(ve[:, u], mv[:, u, :, 1], eps_t[:, 0:UT], ALU.add).then_inc(f_ve, 1)
                    pool.wait_ge(f_ve, n + 1)
                    nc.gpsimd.tensor_tensor(rstd[:, u], ve[:, u], exponent[:, 0:UT],
                                            ALU.pow).then_inc(f_rs, 1)

                for u in range(UNITS):
                    power(n0 + u, u)
                    pool.wait_ge(f_rs, n0 + u + 1)
                    nc.gpsimd.tensor_tensor(rstd_g[:, u], rstd[:, u], gain_t[:, 0:UT], ALU.mult).then_inc(f_rg, 1)

                def slot(k, j, live):
                    if live(0):
                        u = j % UNITS
                        pool.wait_ge(f_t, s0 + k * UNITS + j + 1)
                        nc.gpsimd.tensor_tensor(state[:, u], state[:, u], th[:, j % TR],
                                                ALU.add).then_inc(f_u, 1)
                    if live(2):
                        power(n0 + UNITS + k * UNITS + j - 2, (j - 2) % UNITS)

                scan_slots(pool, SLOTS, UNITS, (0, 2), slot)

        @block.tensor
        def _(pe):
            pe.wait_ge(s_id, 11)
            pe.wait_ge(s_in, 7 * 16)
            for a in range(CB):
                for k in range(CB):
                    last = nc.tensor.transpose(ps[:, 0, k * C + a * P:k * C + (a + 1) * P],
                                               w_raw[:, a, k * P:(k + 1) * P], ident[:])
            last.then_inc(s_wt, 1)
            pe.wait_ge(s_set, 3)
            for k in range(CB):
                last = nc.tensor.matmul(ps[:, 1, 0:C], avg[:], w_s[:, k], start=(k == 0), stop=(k == CB - 1))
            last.then_inc(s_cm, 1)
            for k in range(CB):
                last = nc.tensor.matmul(ps[:, 2, 0:C], lnb_wide[:, k], w_t[:, k], start=(k == 0),
                                        stop=(k == CB - 1))
            last.then_inc(s_cv, 1)
            pe.wait_ge(s_set, SETUP_STEPS)

            def slot(k, j, live):
                first = isinstance(k, int) and k == 0
                if live(-4) and j % 2 == 0:
                    g = (j + 4) // 2
                    r = g % 2
                    pe.wait_ge(s_hn, k * GBODY + g + 1)
                    freed(pe, s_lr, k * GBODY + g - 1)
                    for c in range(CB):
                        for i in range(NB):
                            last = nc.tensor.transpose(ps_t[:, c * N + i * P:c * N + (i + 1) * P],
                                                       hn[:, r, i, c * P:(c + 1) * P], ident[:])
                    last.then_inc(s_hnp, 1)
                if live(-3) and j % 2 == 1:
                    g = (j + 3) // 2
                    r = g % 2
                    pe.wait_ge(s_hnt, k * GBODY + g + 1)
                    freed(pe, s_sdl, k * GBODY + g)
                    for i in range(NB):
                        for c in range(CB):
                            last = nc.tensor.matmul(ps_wh[:, i], hnt[:, r, c, i * P:(i + 1) * P], gw[:, c],
                                                    start=(c == 0), stop=(c == CB - 1))
                    last.then_inc(s_wh, 1)
                if live(-1) and j % 2 == 1:
                    g = (j + 1) // 2
                    pe.wait_ge(s_sdl, k * GBODY + g + 1)
                    if not (isinstance(k, int) and k * GBODY + g + 2 > B):
                        pe.wait_ge(s_hnt, k * GBODY + g + 2)
                    for i in range(NB):
                        for side in range(2):
                            last = nc.tensor.transpose(ps_t[0:16, side * N + i * P:side * N + (i + 1) * P],
                                                       sd[:, i, 4 * side:4 * side + 4], ident[:])
                    last.then_inc(s_lrp, 1)
                if live(1):
                    s, r = j - 1, (j - 1) % 2
                    pe.wait_ge(s_exp, k * HBODY + s + 1)
                    freed(pe, s_et, k * HBODY + s)
                    for h in range(HEADS):
                        for jb in range(NB):
                            col = (h % 2) * N + jb * P
                            last = nc.tensor.transpose(ps_et[:, h // 2, col:col + P],
                                                       em[:, r, h, jb * P:(jb + 1) * P], ident[:])
                    last.then_inc(s_te, 1)
                if live(2):
                    s = j - 2
                    r, i, g4 = s % 2, s % NB, (s // NB) % GBODY
                    pe.wait_ge(s_et, k * HBODY + s + 1)
                    freed(pe, s_att, k * HBODY + s)
                    for h in range(HEADS):
                        for jb in range(NB):
                            last = nc.tensor.matmul(ps_o[:, i * C + h * DH:i * C + (h + 1) * DH],
                                                    ets[:, r, h, jb], wh[:, g4, jb, h * DH:(h + 1) * DH],
                                                    start=(jb == 0), stop=(jb == NB - 1))
                    last.then_inc(s_o, 1)
                if live(-1):
                    s = j + 1
                    g, i = s // NB, s % NB
                    r = g % 2
                    pe.wait_ge(s_rh, k * GBODY + g + 1)
                    freed(pe, s_ttr, k * HBODY + s)
                    for h in range(HEADS):
                        last = nc.tensor.matmul(ps_e[:, h // 2, (h % 2) * N:(h % 2 + 1) * N],
                                                lr[:, r, 0, i * P:(i + 1) * P], rh[:, r, h],
                                                start=True, stop=True)
                    last.then_inc(s_e, 1)

            scan_slots(pe, HALVES, HBODY, (-4, -3, -2, -1, 1, 2), slot, peeled=2)

            with pe.Fori(0, BATCHES) as b:
                s0 = b * SLOTS
                n0 = b * NORMS

                def slot(k, j, live):
                    first = isinstance(k, int) and k == 0
                    m0 = s0 + k * UNITS
                    if live(1):
                        m = j - 1
                        q = (m % 2) * 2
                        pe.wait_ge(f_g, m0 + m + 1)
                        if not (first and m < 2):
                            pe.wait_ge(f_tc, m0 + m - 1)
                        for c in range(CB):
                            for t in range(UT):
                                last = nc.tensor.transpose(ps[:, q + c, t * P:(t + 1) * P],
                                                           state[:, m % UNITS, t * C + c * P:t * C + (c + 1) * P],
                                                           ident[:])
                        last.then_inc(f_tp, 1)
                    if live(3):
                        m = j - 3
                        q = 4 + (m % 2) * 2
                        pe.wait_ge(f_tc, m0 + m + 1)
                        if not (first and m < 2):
                            pe.wait_ge(f_z, n0 + k * UNITS + UNITS + m - 1)
                        for t in range(UT):
                            for c in range(CB):
                                last = nc.tensor.matmul(ps[:, q + t // 2, (t % 2) * C:(t % 2 + 1) * C],
                                                        gts[:, m % GR, c, t * P:(t + 1) * P], w_c[:, c],
                                                        start=(c == 0), stop=(c == CB - 1))
                        last.then_inc(f_mm, 1)

                scan_slots(pe, SLOTS, UNITS, (1, 3), slot)

        @block.scalar
        def _(act):
            def slot(k, j, live):
                first = isinstance(k, int) and k == 0
                if live(-4) and j % 2 == 0:
                    g = (j + 4) // 2
                    r = g % 2
                    act.wait_ge(s_hnp, k * GBODY + g + 1)
                    freed(act, s_wh, k * GBODY + g - 1)
                    nc.scalar.activation(hnt[:, r], ps_t.rearrange("p (c n) -> p c n", c=CB),
                                         ACT.Copy).then_inc(s_hnt, 1)
                if live(-2) and j % 2 == 0:
                    g = (j + 2) // 2
                    act.wait_ge(s_wh, k * GBODY + g + 1)
                    freed(act, s_o, k * HBODY + 2 * (g - GBODY) + 2)
                    nc.scalar.activation(wh[:, g % GBODY], ps_wh[:, :, 0:C], ACT.Copy).then_inc(s_whc, 1)
                    freed(act, s_lrp, k * GBODY + g)
                    nc.scalar.activation(sd[:, :, 0:8:6].bitcast(F32R),
                                         ps_wh[:, :, C:C + SD].rearrange("p i (a h) -> p i a h", a=2),
                                         ACT.Copy).then_inc(s_sdh, 1)
                if live(-1) and j % 2 == 1:
                    g = (j + 1) // 2
                    r = g % 2
                    act.wait_ge(s_lrp, k * GBODY + g + 1)
                    freed(act, s_e, k * HBODY + 2 * g - 2)
                    freed(act, s_rh, k * GBODY + g - 1)
                    nc.scalar.activation(lr[:, r], ps_t[0:16].rearrange("p (a n) -> p a n", a=2),
                                         ACT.Copy).then_inc(s_lr, 1)
                if live(1):
                    s, r = j - 1, (j - 1) % 2
                    act.wait_ge(s_te, k * HBODY + s + 1)
                    freed(act, s_o, k * HBODY + s - 1)
                    nc.scalar.activation(ets[:, r].rearrange("p (a h) i n -> p a (h i n)", a=2), ps_et[:],
                                         ACT.Copy).then_inc(s_et, 1)
                if live(0):
                    s, r = j, j % 2
                    act.wait_ge(s_l, k * HBODY + s + 1)
                    act.wait_ge(s_nmx, k * HBODY + s + 1)
                    freed(act, s_rcp, k * HBODY + s - 3)
                    for h in range(HEADS):
                        last = nc.scalar.activation(em[:, r, h], em[:, r, h], ACT.Exp, bias=nmx[:, r, h:h + 1],
                                                    accum_out=rs[:, s % 4, h:h + 1])
                    last.then_inc(s_exp, 1)
                if live(6) and j % 2 == 0:
                    g = (j - 6) // 2
                    r = g % 2
                    act.wait_ge(s_neg, k * GBODY + g + 1)
                    nc.scalar.activation(neg[:, r], neg[:, r], ACT.Exp).then_inc(s_ex, 1)

            scan_slots(act, HALVES, HBODY, (-4, -2, -1, 0, 1, 6), slot, peeled=2)

            with act.Fori(0, BATCHES) as b:
                s0 = b * SLOTS
                n0 = b * NORMS

                def slot(k, j, live):
                    first = isinstance(k, int) and k == 0
                    m0 = s0 + k * UNITS
                    if live(2):
                        m = j - 2
                        q = (m % 2) * 2
                        act.wait_ge(f_tp, m0 + m + 1)
                        if not (first and m < GR):
                            act.wait_ge(f_mm, m0 + m - GR + 1)
                        nc.scalar.activation(gts[:, m % GR], ps[:, q:q + 2], ACT.Copy).then_inc(f_tc, 1)
                    if live(1):
                        m = j - 1
                        act.wait_ge(f_u, m0 + m + 1)
                        nc.scalar.activation(state[:, m % UNITS], state[:, m % UNITS], ACT.Silu,
                                             scale=1.0 / GAIN).then_inc(f_g, 1)
                    if live(0):
                        m = j
                        act.wait_ge(f_z, n0 + k * UNITS + m + 1)
                        if not (first and m < TR):
                            act.wait_ge(f_u, m0 + m - TR + 1)
                        nc.scalar.activation(th[:, m % TR], state[:, m % UNITS], ACT.Tanh,
                                             scale=1.0 / GAIN).then_inc(f_t, 1)

                scan_slots(act, SLOTS, UNITS, (0, 1, 2), slot)

        @block.vector
        def _(dve):
            V = nc.vector
            done = [0]

            def step(ins):
                done[0] += 1
                ins.then_inc(s_set, 1)
                return done[0]

            dve.wait_ge(s_wt, 1)
            step(V.tensor_copy(w_t[:], ps[:, 0].rearrange("p (k c) -> p k c", k=CB)))
            dve.wait_ge(s_set, 1)
            for k in range(CB):
                last = V.tensor_scalar(w_s[:, k], w_t[:, k], lnw[:, k:k + 1], GAIN, ALU.mult, ALU.mult)
            step(last)
            dve.wait_ge(s_id, 11)
            for k in range(CB):
                last = V.tensor_scalar(lnb_wide[:, k], avg[:], 0.0, lnb[:, k:k + 1], ALU.mult, ALU.add)
            step(last)
            dve.wait_ge(s_cm, 1)
            for k in range(CB):
                last = V.tensor_tensor(w_c[:, k], w_s[:, k], ps[:, 1, 0:C], ALU.subtract)
            step(last)
            dve.wait_ge(s_cv, 1)
            n = step(V.tensor_tensor(c_sum[:], ps[:, 2, 0:C], b_bc[:], ALU.add))
            dve.wait_ge(s_set, n)
            step(V.tensor_scalar(c_bc[:], c_sum[:], GAIN, None, ALU.mult))
            for k in range(CB):
                for side in range(2):
                    n = step(V.tensor_tensor(prod[:], gw[:, k, 0:C].rearrange("p (h d) -> p h d", h=HEADS),
                                             a_bc[:, :, side], ALU.mult))
                    dve.wait_ge(s_set, n)
                    n = step(V.tensor_reduce(gw[:, k, C + HEADS * side:C + HEADS * (side + 1)], prod[:], AX.X,
                                             ALU.add))
                    dve.wait_ge(s_set, n)
            step(V.tensor_scalar(mask[:], adj_i[:], 0.0, MASKED, ALU.is_equal, ALU.mult))
            n = step(V.tensor_scalar(edge[:], adj_i[:], 0.0, None, ALU.not_equal))
            dve.wait_ge(s_set, n)
            step(V.tensor_reduce(has_edge[:], edge[:], AX.X, ALU.max))
            step(V.memset(sd[:], 1.0))
            assert done[0] == SETUP_STEPS

            def slot(k, j, live):
                first = isinstance(k, int) and k == 0
                g0, h0 = k * GBODY, k * HBODY
                if live(0):
                    s, r = j, j % 2
                    dve.wait_ge(s_e, h0 + s + 1)
                    freed(dve, s_te, h0 + s - 1)
                    freed(dve, s_mxl, h0 + s - 1)
                    dve.sem_inc(passed["dve"], 1)
                    for h in range(HEADS):
                        last = V.tensor_tensor_reduce(out=em[:, r, h],
                                                      in0=ps_e[:, h // 2, (h % 2) * N:(h % 2 + 1) * N],
                                                      in1=mask[:, s % NB], scale=1.0, scalar=-3e38,
                                                      op0=ALU.add, op1=ALU.max, accum_out=mx[:, r, h:h + 1])
                    last.then_inc(s_ttr, 1)
                if live(3):
                    s = j - 3
                    i, g4 = s % NB, (s // NB) % GBODY
                    dve.wait_ge(s_o, h0 + s + 1)
                    dve.wait_ge(s_rn, h0 + s + 1)
                    freed(dve, s_el, g0 + s // NB - GBODY + 1)
                    V.tensor_tensor(att[:, g4, i].rearrange("p (h d) -> p h d", h=HEADS),
                                    ps_o[:, i * C:(i + 1) * C].rearrange("p (h d) -> p h d", h=HEADS),
                                    rnorm[:, s % 4].unsqueeze(2).to_broadcast([P, HEADS, DH]),
                                    ALU.mult).then_inc(s_att, 1)
                if live(0):
                    s, r = j, j % 2
                    dve.wait_ge(s_ttr, h0 + s + 1)
                    V.scalar_tensor_tensor(mxl[:, r], mx[:, r], SLOPE, mx[:, r], ALU.mult,
                                           ALU.max).then_inc(s_mxl, 1)
                    V.scalar_tensor_tensor(em[:, r].rearrange("p h n -> p (h n)"),
                                           em[:, r].rearrange("p h n -> p (h n)"), SLOPE,
                                           em[:, r].rearrange("p h n -> p (h n)"), ALU.mult,
                                           ALU.max).then_inc(s_l, 1)
                    dve.wait_ge(s_mxl, h0 + s + 1)
                    freed(dve, s_exp, h0 + s - 1)
                    V.tensor_scalar(nmx[:, r], mxl[:, r], -1.0, None, ALU.mult).then_inc(s_nmx, 1)
                if live(7) and j % 2 == 1:
                    g = (j - 7) // 2
                    r = g % 2
                    dve.wait_ge(s_ex, g0 + g + 1)
                    V.scalar_tensor_tensor(neg[:, r].rearrange("p i c -> p (i c)"),
                                           att[:, g % GBODY].rearrange("p i c -> p (i c)"), 0.0,
                                           neg[:, r].rearrange("p i c -> p (i c)"), ALU.max,
                                           ALU.add).then_inc(s_el, 1)
                if live(4) and j % 2 == 0:
                    g = (j - 4) // 2
                    r = g % 2
                    dve.wait_ge(s_att, h0 + 2 * g + 2)
                    freed(dve, s_x1, g0 + g - 1)
                    V.tensor_scalar(neg[:, r], att[:, g % GBODY], 0.0, None, ALU.min).then_inc(s_neg, 1)
                if live(-6) and j % 2 == 0:
                    g = (j + 6) // 2
                    r = g % 2
                    dve.wait_ge(s_xin[r], 16 * (2 * k + g // 2 + 1))
                    freed(dve, s_hn, g0 + g - 1)
                    for i in range(NB):
                        last = V.bn_stats(g_st[:, r, i], xin[:, r, i])
                    last.then_inc(s_gbn, 1)
                    dve.wait_ge(s_gbn, g0 + g + 1)
                    dve.sem_inc(passed["dve"], 1)
                    for i in range(NB):
                        last = V.bn_aggr(g_mv[:, r, i], g_st[:, r, i])
                    last.then_inc(s_gmv, 1)
                if live(-5) and j % 2 == 1:
                    g = (j + 5) // 2
                    r = g % 2
                    dve.wait_ge(s_grs, g0 + g + 1)
                    freed(dve, s_hnp, g0 + g - 1)
                    for i in range(NB):
                        last = V.tensor_scalar(hn[:, r, i], xin[:, r, i], g_mv[:, r, i, 0:1],
                                               g_rstd[:, r, i:i + 1], ALU.subtract, ALU.mult)
                    last.then_inc(s_hn, 1)
                if live(-2) and j % 2 == 0:
                    g = (j + 2) // 2
                    dve.wait_ge(s_sdh, g0 + g + 1)
                    V.tensor_tensor(sd[:, :, 1:8:6].bitcast(F32R),
                                    ps_wh[:, :, C:C + SD].rearrange("p i (a h) -> p i a h", a=2),
                                    sd[:, :, 0:8:6], ALU.subtract).then_inc(s_sdl, 1)
                if live(1):
                    s = j - 1
                    dve.wait_ge(s_exp, h0 + s + 1)
                    freed(dve, s_rn, h0 + s - 1)
                    V.reciprocal(rcp[:, s % 2], rs[:, s % 4]).then_inc(s_rcp, 1)
                    dve.wait_ge(s_rcp, h0 + s + 1)
                    freed(dve, s_att, h0 + s - 3)
                    V.tensor_scalar(rnorm[:, s % 4], rcp[:, s % 2], has_edge[:, s % NB:s % NB + 1], None,
                                    ALU.mult).then_inc(s_rn, 1)
                if live(7) and j % 2 == 1:
                    g = (j - 7) // 2
                    r = g % 2
                    dve.wait_ge(s_el, g0 + g + 1)
                    dve.wait_ge(s_xres[r], 16 * (2 * k + g // 2 + 1))
                    V.scalar_tensor_tensor(xres[:, r].rearrange("p i c -> p (i c)"),
                                           neg[:, r].rearrange("p i c -> p (i c)"), -1.0,
                                           xres[:, r].rearrange("p i c -> p (i c)"), ALU.add,
                                           ALU.add).then_inc(s_x1, 1)

            scan_slots(dve, HALVES, HBODY, (-6, -5, -2, 0, 1, 3, 4, 7), slot, peeled=2)

            with dve.Fori(0, BATCHES) as b:
                n0 = b * NORMS
                s0 = b * SLOTS

                def stats(n, u, src):
                    for t in range(UT):
                        last = V.bn_stats(st[:, u, t], src[:, u, t * C:(t + 1) * C])
                    last.then_inc(f_bn, 1)
                    dve.wait_ge(f_bn, n + 1)
                    dve.sem_inc(passed["dve"], 1)
                    for t in range(UT):
                        last = V.bn_aggr(mv[:, u, t], st[:, u, t])
                    last.then_inc(f_mv, 1)

                def normalise(u):
                    dve.wait_ge(f_rg, b * UNITS + u + 1)
                    for t in range(UT):
                        last = V.tensor_scalar(state[:, u, t * C:(t + 1) * C], x1_sb[:, u, t * C:(t + 1) * C],
                                               mv[:, u, t, 0:1], rstd_g[:, u, t:t + 1], ALU.subtract, ALU.mult)
                    last.then_inc(f_z, 1)

                for u in range(UNITS):
                    dve.wait_ge(f_ld[u], b * 16 + 16)
                    stats(n0 + u, u, x1_sb)
                    if u >= 1:
                        normalise(u - 1)
                normalise(UNITS - 1)

                def slot(k, j, live):
                    m0 = s0 + k * UNITS
                    if live(4):
                        m = j - 4
                        u, q = m % UNITS, 4 + (m % 2) * 2
                        dve.wait_ge(f_mm, m0 + m + 1)
                        dve.wait_ge(f_rs, n0 + k * UNITS + UNITS + m + 1)
                        for t in range(UT):
                            last = V.scalar_tensor_tensor(state[:, u, t * C:(t + 1) * C],
                                                          ps[:, q + t // 2, (t % 2) * C:(t % 2 + 1) * C],
                                                          rstd[:, u, t:t + 1], c_bc[:], ALU.mult, ALU.add)
                        last.then_inc(f_z, 1)
                    if live(1):
                        m = j - 1
                        dve.wait_ge(f_g, m0 + m + 1)
                        stats(n0 + UNITS + k * UNITS + m, m % UNITS, state)

                scan_slots(dve, SLOTS, UNITS, (1, 4), slot)
                for u in range(UNITS):
                    dve.wait_ge(f_z, n0 + SLOTS + u + 1)
                    V.scalar_tensor_tensor(x1_sb[:, u], state[:, u], 1.0 / GAIN, x1_sb[:, u], ALU.mult,
                                           ALU.add).then_inc(f_out, 1)


def kernel(**inputs):
    import concourse.bacc as bacc
    from concourse.bass_utils import run_bass_kernel_spmd

    nc = bacc.Bacc("TRN2", target_bir_lowering=False, num_devices=1)
    names = ["x", "adj", "L0_gnn_W", "L0_gnn_a", "L0_ffn_ln_w", "L0_ffn_ln_b", "L0_ffn_W", "L0_ffn_b"]
    arrays, args = {}, []
    for name in names:
        a = np.ascontiguousarray(inputs[name])
        if name == "x":
            a = a.reshape(ROWS, C)
        arrays["in_" + name] = a
        args.append(nc.dram_tensor("in_" + name, a.shape, mybir.dt.from_np(a.dtype), kind="ExternalInput").ap())
    x1 = nc.dram_tensor("x1_scratch", (ROWS, C), F32, kind="Internal").ap()
    out = nc.dram_tensor("out", (ROWS, C), F32, kind="ExternalOutput").ap()
    build(nc, *args, x1, out)
    r = run_bass_kernel_spmd(nc, [arrays], core_ids=[0])
    return r.results[0]["out"].reshape(B, N, C)
```

```python
import concourse.bass as bass
import concourse.mybir as mybir
from contextlib import ExitStack
import numpy as np

F32 = mybir.dt.float32
F32R = mybir.dt.float32r
I32 = mybir.dt.int32
ALU = mybir.AluOpType
ACT = mybir.ActivationFunctionType
AX = mybir.AxisListType

P = 128
B, N, C = 64, 256, 256
HEADS, DH = 4, 64
NB = N // P
CB = C // P
EPS = 1e-5
SLOPE = 0.2
STEPS = 30
GAIN = 100.0
MASKED = -1e30

GBODY = 4
HBODY = NB * GBODY
HALVES = NB * B
SD = 2 * HEADS

UT = 4
UNITS = 8
UF = UT * C
HT = UT // 2
ROWS = B * N
BATCHES = ROWS // (P * UT * UNITS)
SLOTS = BATCHES * STEPS * UNITS


SETUP_STEPS = 3 + 5 + 4 * CB + 4


def freed(eng, sem, count):
    if not (isinstance(count, int) and count <= 0):
        eng.wait_ge(sem, count)


def scan_slots(eng, total, body, lags, slot, peeled=1):
    low, high = min(lags), max(lags)
    assert high <= peeled * body
    stop = (total + low) // body if low < 0 else total // body
    for s in range(low, peeled * body):
        k = max(s, 0) // body
        slot(k, s - k * body, lambda l, s=s: 0 <= s - l < total)
    with eng.Fori(peeled, stop) as k:
        for j in range(body):
            slot(k, j, lambda l: True)
    for s in range(stop * body, total + high):
        slot(stop, s - stop * body, lambda l, s=s: 0 <= s - l < total)


def build(nc, x, adj, gnn_w, gnn_a, ln_w, ln_b, ffn_w, ffn_b, x1, out):
    ctx = ExitStack()
    with ctx:
        def sb(name, shape, dt=F32):
            return ctx.enter_context(nc.sbuf_tensor(name, shape, dt))

        def sem(name):
            return ctx.enter_context(nc.semaphore(name))

        ident = sb("ident", [P, P])
        avg = sb("avg", [P, P])
        exponent = sb("exponent", [P, 8])
        eps_t = sb("eps_t", [P, 8])
        gain_t = sb("gain_t", [P, 8])
        gw = sb("gw", [P, CB, C + SD])
        a_bc = sb("a_bc", [P, HEADS, 2, DH])
        prod = sb("prod", [P, HEADS, DH])
        adj_i = sb("adj_i", [P, NB, N], I32)
        mask = sb("mask", [P, NB, N])
        edge = sb("edge", [P, NB, N])
        has_edge = sb("has_edge", [P, NB])
        head_rows = sb("head_rows", [16, HEADS])
        w_raw = sb("w_raw", [P, CB, C])
        w_t = sb("w_t", [P, CB, C])
        w_s = sb("w_s", [P, CB, C])
        w_c = sb("w_c", [P, CB, C])
        w_hi = sb("w_hi", [P, CB, C], F32R)
        w_lo = sb("w_lo", [P, CB, C], F32R)
        lnw = sb("lnw", [P, CB])
        lnb = sb("lnb", [P, CB])
        lnb_wide = sb("lnb_wide", [P, CB, P])
        b_bc = sb("b_bc", [P, C])
        c_sum = sb("c_sum", [P, C])
        c_bc = sb("c_bc", [P, C])
        xin = sb("xin", [P, 2, NB, C])
        xres = sb("xres", [P, 2, NB, C])
        g_st = sb("g_st", [P, 2, NB, 6])
        g_mv = sb("g_mv", [P, 2, NB, 2])
        g_ve = sb("g_ve", [P, 2, NB])
        g_rstd = sb("g_rstd", [P, 2, NB])
        hn = sb("hn", [P, 2, NB, C])
        hnt = sb("hnt", [P, 2, CB, N])
        sd = sb("sd", [P, NB, 8, 4])
        lr = sb("lr", [16, 2, 2, N], F32R)
        rh = sb("rh", [16, 2, HEADS, N], F32R)
        mx = sb("mx", [P, 2, HEADS])
        mxl = sb("mxl", [P, 2, HEADS])
        nmx = sb("nmx", [P, 2, HEADS])
        rs = sb("rs", [P, 4, HEADS])
        rcp = sb("rcp", [P, 2, HEADS])
        rnorm = sb("rnorm", [P, 4, HEADS])
        neg = sb("neg", [P, 2, NB, C])
        x_st = sb("x_st", [P, 2, NB, 6])
        x_mv2 = sb("x_mv2", [P, 2, NB, 2])
        x_ve = sb("x_ve", [P, 2, NB])
        x_rs = sb("x_rs", [P, 2, NB])
        x_mv = sb("x_mv", [P, HALVES, 2])
        x_rstd = sb("x_rstd", [P, HALVES])
        x1_sb = sb("x1_sb", [P, 2, UNITS, UF])
        st = sb("st", [P, UNITS, UT, 6])
        mv = sb("mv", [P, UNITS, UT, 2])
        ve = sb("ve", [P, UNITS, UT])
        rstd = sb("rstd", [P, UNITS, UT])
        state = sb("state", [P, UNITS, UF])
        flat = state[:, :, :].rearrange("p u f -> p (u f)")
        Q = UNITS * UF // 4
        wh = flat[:, 0:Q].rearrange("p (g i c) -> p g i c", g=GBODY, i=NB)
        ER = 4
        em = x1_sb[:, 0].rearrange("p u f -> p (u f)")[:, 0:ER * HEADS * N].rearrange(
            "p (r h n) -> p r h n", r=ER, h=HEADS)
        ets = flat[:, 2 * Q:3 * Q].rearrange("p (r h i n) -> p r h i n", r=2, h=HEADS, i=NB)
        att = flat[:, 3 * Q:4 * Q].rearrange("p (g i c) -> p g i c", g=GBODY, i=NB)
        TR = 4
        th = sb("th", [P, TR, UF])
        GR = 4
        g_f = sb("g_f", [P, GR, CB, HT * P])
        g_hi = sb("g_hi", [P, GR, CB, HT * P], F32R)
        g_lo = sb("g_lo", [P, GR, CB, HT * P], F32R)
        ps = ctx.enter_context(nc.psum_tensor("ps", [P, 8, 512], F32))

        ps_t = ps[:, 0, :]
        ps_wh = ps[:, 1:3, 0:C + SD]
        ps_e = ps[:, 3:5, :]
        ps_o = ps[:, 5, :]
        ps_et = ps[:, 6:8, :]

        s_in = sem("weights_loaded")
        s_id = sem("ident_ready")
        s_set = sem("setup_dve")
        s_wt = sem("w_transposed")
        s_cm = sem("colmean_ready")
        s_cv = sem("c_ready")
        s_xin = [sem(f"xin_loaded{r}") for r in range(2)]
        s_xres = [sem(f"xres_loaded{r}") for r in range(2)]
        s_x1st = [sem(f"x1_stored{r}") for r in range(2)]
        s_gbn = sem("g_bn")
        s_gmv = sem("g_meanvar")
        s_gve = sem("g_ve")
        s_grs = sem("g_rstd")
        s_hn = sem("hn_ready")
        s_hnp = sem("hn_transposed")
        s_hnt = sem("hnt_copied")
        s_wh = sem("wh_done")
        s_whc = sem("wh_copied")
        s_sdh = sem("sd_hi")
        s_sdl = sem("sd_lo")
        s_lrp = sem("lr_transposed")
        s_lr = sem("lr_copied")
        s_rh = sem("rh_ready")
        s_e = sem("scores_ready")
        s_ttr = sem("scores_masked")
        s_mxl = sem("max_lrelu")
        s_nmx = sem("neg_max")
        s_l = sem("lrelu_done")
        s_exp = sem("exp_done")
        s_te = sem("probs_transposed")
        s_et = sem("probs_copied")
        s_o = sem("attended")
        s_rcp = sem("rcp_ready")
        s_rn = sem("rnorm_ready")
        s_att = sem("att_ready")
        s_neg = sem("neg_ready")
        s_ex = sem("elu_exp")
        s_el = sem("elu_sum")
        s_x1 = sem("x1_ready")
        s_xbn = sem("x1_bn")
        s_xmv = sem("x1_meanvar")
        s_xve = sem("x1_ve")
        s_xmc = sem("x1_mean_copied")
        s_xrs = sem("x1_rstd")
        s_xrg = sem("x1_rstd_gain")
        f_ld = [[sem(f"f_loaded{p}_{u}") for u in range(UNITS)] for p in range(2)]
        f_st = [sem(f"f_stored{u}") for u in range(UNITS)]
        f_bn = sem("f_bn")
        f_mv = sem("f_meanvar")
        f_ve = sem("f_ve")
        f_rs = sem("f_rstd")
        f_lo = sem("g_lo_ready")
        f_z = sem("state_ready")
        f_t = sem("tanh_done")
        f_u = sem("sum_done")
        f_g = sem("silu_done")
        f_tp = sem("g_transposed")
        f_tc = sem("gt_copied")
        f_mm = sem("product_done")
        f_end = sem("last_state")
        f_out = sem("out_ready")
        passed = {e: sem(f"passed_{e}") for e in ("sp", "dve")}

        block = ctx.enter_context(nc.Block())

        def graph(t, k, j):
            g = k * GBODY + j
            return t.rearrange("(g i p) c -> g p i c", i=NB, p=P)[g]

        def unit(t, b, u):
            return t.rearrange("(b u t p) c -> b u p t c", u=UNITS, p=P, t=UT)[b, u]

        def tiles(t, buf, u):
            return t[:, buf, u].rearrange("p (t c) -> p t c", t=UT)

        @block.sync
        def _(sp):
            sp.dma_start(gw[:, :, 0:C], gnn_w.rearrange("(k p) c -> p k c", p=P)).then_inc(s_in, 16)
            sp.dma_start(a_bc[:], gnn_a.rearrange("h (two d) -> h two d", two=2).unsqueeze(0)
                         .to_broadcast([P, HEADS, 2, DH])).then_inc(s_in, 16)
            sp.dma_start(adj_i[:], adj.rearrange("(i p) j -> p i j", p=P)).then_inc(s_in, 16)
            sp.dma_start(w_raw[:], ffn_w.rearrange("(k p) c -> p k c", p=P)).then_inc(s_in, 16)
            sp.dma_start(b_bc[:], ffn_b.unsqueeze(0).to_broadcast([P, C])).then_inc(s_in, 16)
            sp.dma_start(lnw[:], ln_w.rearrange("(k p) -> p k", p=P),
                         allow_slow_non_contiguous=True).then_inc(s_in, 16)
            sp.dma_start(lnb[:], ln_b.rearrange("(k p) -> p k", p=P),
                         allow_slow_non_contiguous=True).then_inc(s_in, 16)

            def slot(k, j, live):
                if live(-7):
                    g, r = j + 7, (j + 7) % 2
                    freed(sp, s_hn, k * GBODY + g - 1)
                    sp.sem_inc(passed["sp"], 1)
                    sp.dma_start(xin[:, r], graph(x, k, g)).then_inc(s_xin[r], 16)
                if live(0):
                    g, r = j, j % 2
                    freed(sp, s_xmv, k * GBODY + g - 1)
                    sp.sem_inc(passed["sp"], 1)
                    freed(sp, s_x1st[r], 16 * (2 * k + g // 2))
                    sp.sem_inc(passed["sp"], 1)
                    sp.dma_start(xres[:, r], graph(x, k, g)).then_inc(s_xres[r], 16)
                if live(1):
                    g, r = j - 1, (j - 1) % 2
                    sp.wait_ge(s_x1, k * GBODY + g + 1)
                    sp.sem_inc(passed["sp"], 1)
                    sp.dma_start(graph(x1, k, g), xres[:, r]).then_inc(s_x1st[r], 16)

            scan_slots(sp, B, GBODY, (-7, 0, 1), slot, peeled=2)
            for r in range(2):
                sp.wait_ge(s_x1st[r], 16 * (B // 2))
            for b in range(BATCHES + 1):
                if b < BATCHES:
                    for u in range(UNITS):
                        if b >= 2:
                            sp.wait_ge(f_st[u], 16 * (b - 1))
                        sp.dma_start(tiles(x1_sb, b % 2, u), unit(x1, b, u)).then_inc(f_ld[b % 2][u], 16)
                if b >= 1:
                    for u in range(UNITS):
                        sp.wait_ge(f_out, (b - 1) * UNITS + u + 1)
                        sp.dma_start(unit(out, b - 1, u), tiles(x1_sb, (b - 1) % 2, u)).then_inc(f_st[u], 16)
            for u in range(UNITS):
                sp.wait_ge(f_st[u], 16 * BATCHES)

        @block.gpsimd
        def _(pool):
            nc.gpsimd.memset(ident[:], 0.0).then_inc(s_id, 1)
            nc.gpsimd.memset(head_rows[:], 0.0).then_inc(s_id, 1)
            pool.wait_ge(s_id, 2)
            nc.gpsimd.affine_select(out=ident[:], in_=ident[:], compare_op=ALU.not_equal, fill=1.0, base=0,
                                    pattern=[[-1, P]], channel_multiplier=1).then_inc(s_id, 1)
            for q in range(4):
                pool.wait_ge(s_id, 3 + q)
                nc.gpsimd.affine_select(out=head_rows[:], in_=head_rows[:], compare_op=ALU.not_equal,
                                        fill=1.0, base=-HEADS * q, pattern=[[-1, HEADS]],
                                        channel_multiplier=1).then_inc(s_id, 1)
            nc.gpsimd.memset(exponent[:], -0.5).then_inc(s_id, 1)
            nc.gpsimd.memset(eps_t[:], EPS).then_inc(s_id, 1)
            nc.gpsimd.memset(gain_t[:], GAIN).then_inc(s_id, 1)
            nc.gpsimd.memset(avg[:], 1.0 / C).then_inc(s_id, 1)
            pool.wait_ge(s_id, 11)

            def slot(k, j, live):
                if live(-2) and j % 2 == 0:
                    g = (j + 2) // 2
                    r = g % 2
                    pool.wait_ge(s_lr, k * GBODY + g + 1)
                    freed(pool, s_e, k * HBODY + 2 * g - 2)
                    for h in range(HEADS):
                        last = nc.gpsimd.tensor_tensor(rh[:, r, h], lr[:, r, 1].bitcast(F32),
                                                       head_rows[:, h:h + 1].to_broadcast([16, N]), ALU.mult)
                    last.then_inc(s_rh, 1)
                if live(8) and j % 2 == 0:
                    g = (j - 8) // 2
                    r = g % 2
                    pool.wait_ge(s_el, k * GBODY + g + 1)
                    nc.gpsimd.tensor_tensor(xres[:, r], xres[:, r], att[:, g % GBODY], ALU.add).then_inc(s_x1, 1)
                if live(-8) and j % 2 == 0:
                    g = (j + 8) // 2
                    r = g % 2
                    pool.wait_ge(s_gmv, k * GBODY + g + 1)
                    nc.gpsimd.tensor_tensor(g_ve[:, r], g_mv[:, r, :, 1], eps_t[:, 0:NB],
                                            ALU.add).then_inc(s_gve, 1)
                    pool.wait_ge(s_gve, k * GBODY + g + 1)
                    nc.gpsimd.tensor_tensor(g_rstd[:, r], g_ve[:, r], exponent[:, 0:NB],
                                            ALU.pow).then_inc(s_grs, 1)
                if live(7) and j % 2 == 1:
                    g = (j - 7) // 2
                    r = g % 2
                    pool.wait_ge(s_neg, k * GBODY + g + 1)
                    pool.wait_ge(s_xres[r], 16 * (2 * k + g // 2 + 1))
                    nc.gpsimd.tensor_tensor(xres[:, r], xres[:, r], neg[:, r], ALU.add).then_inc(s_el, 1)
                if live(9) and j % 2 == 1:
                    g = (j - 9) // 2
                    r = g % 2
                    pool.wait_ge(s_xmv, k * GBODY + g + 1)
                    nc.gpsimd.tensor_copy(x_mv[:, bass.ds(k * HBODY + 2 * g, NB)], x_mv2[:, r]).then_inc(s_xmc, 1)
                    nc.gpsimd.tensor_tensor(x_ve[:, r], x_mv2[:, r, :, 1], eps_t[:, 0:NB],
                                            ALU.add).then_inc(s_xve, 1)
                    pool.wait_ge(s_xve, k * GBODY + g + 1)
                    nc.gpsimd.tensor_tensor(x_rs[:, r], x_ve[:, r], exponent[:, 0:NB],
                                            ALU.pow).then_inc(s_xrs, 1)
                    pool.wait_ge(s_xrs, k * GBODY + g + 1)
                    nc.gpsimd.tensor_tensor(x_rstd[:, bass.ds(k * HBODY + 2 * g, NB)], x_rs[:, r],
                                            gain_t[:, 0:NB], ALU.mult).then_inc(s_xrg, 1)

            scan_slots(pool, HALVES, HBODY, (-8, -2, 7, 8, 9), slot, peeled=2)

            def slot(k, j, live):
                if live(0):
                    u = j % UNITS
                    pool.wait_ge(f_t, k * UNITS + j + 1)
                    nc.gpsimd.tensor_tensor(state[:, u], state[:, u], th[:, j % TR], ALU.add).then_inc(f_u, 1)
                if live(2):
                    n, u = k * UNITS + j - 2, (j - 2) % UNITS
                    pool.wait_ge(f_mv, n + 1)
                    nc.gpsimd.tensor_tensor(ve[:, u], mv[:, u, :, 1], eps_t[:, 0:UT], ALU.add).then_inc(f_ve, 1)
                    pool.wait_ge(f_ve, n + 1)
                    nc.gpsimd.tensor_tensor(rstd[:, u], ve[:, u], exponent[:, 0:UT],
                                            ALU.pow).then_inc(f_rs, 1)

            scan_slots(pool, SLOTS, UNITS, (0, 2), slot)

        @block.tensor
        def _(pe):
            pe.wait_ge(s_id, 11)
            pe.wait_ge(s_in, 7 * 16)
            for a in range(CB):
                for k in range(CB):
                    last = nc.tensor.transpose(ps[:, 0, k * C + a * P:k * C + (a + 1) * P],
                                               w_raw[:, a, k * P:(k + 1) * P], ident[:])
            last.then_inc(s_wt, 1)
            pe.wait_ge(s_set, 3)
            for k in range(CB):
                last = nc.tensor.matmul(ps[:, 1, 0:C], avg[:], w_s[:, k], start=(k == 0), stop=(k == CB - 1))
            last.then_inc(s_cm, 1)
            for k in range(CB):
                last = nc.tensor.matmul(ps[:, 2, 0:C], lnb_wide[:, k], w_t[:, k], start=(k == 0),
                                        stop=(k == CB - 1))
            last.then_inc(s_cv, 1)
            pe.wait_ge(s_set, SETUP_STEPS)

            def slot(k, j, live):
                if live(2):
                    s, r = j - 2, (j - 2) % ER
                    pe.wait_ge(s_exp, k * HBODY + s + 1)
                    freed(pe, s_et, k * HBODY + s)
                    for h in range(HEADS):
                        for jb in range(NB):
                            col = (h % 2) * N + jb * P
                            last = nc.tensor.transpose(ps_et[:, h // 2, col:col + P],
                                                       em[:, r, h, jb * P:(jb + 1) * P], ident[:])
                    last.then_inc(s_te, 1)
                if live(-1):
                    s = j + 1
                    g, i = s // NB, s % NB
                    r = g % 2
                    pe.wait_ge(s_rh, k * GBODY + g + 1)
                    freed(pe, s_ttr, k * HBODY + s)
                    for h in range(HEADS):
                        last = nc.tensor.matmul(ps_e[:, h // 2, (h % 2) * N:(h % 2 + 1) * N],
                                                lr[:, r, 0, i * P:(i + 1) * P], rh[:, r, h],
                                                start=True, stop=True)
                    last.then_inc(s_e, 1)
                if live(3):
                    s = j - 3
                    r, i, g4 = s % 2, s % NB, (s // NB) % GBODY
                    pe.wait_ge(s_et, k * HBODY + s + 1)
                    freed(pe, s_att, k * HBODY + s)
                    for h in range(HEADS):
                        for jb in range(NB):
                            last = nc.tensor.matmul(ps_o[:, i * C + h * DH:i * C + (h + 1) * DH],
                                                    ets[:, r, h, jb], wh[:, g4, jb, h * DH:(h + 1) * DH],
                                                    start=(jb == 0), stop=(jb == NB - 1))
                    last.then_inc(s_o, 1)
                if live(-6) and j % 2 == 0:
                    g = (j + 6) // 2
                    r = g % 2
                    pe.wait_ge(s_hn, k * GBODY + g + 1)
                    freed(pe, s_lr, k * GBODY + g - 1)
                    for c in range(CB):
                        for i in range(NB):
                            last = nc.tensor.transpose(ps_t[:, c * N + i * P:c * N + (i + 1) * P],
                                                       hn[:, r, i, c * P:(c + 1) * P], ident[:])
                    last.then_inc(s_hnp, 1)
                if live(-3) and j % 2 == 1:
                    g = (j + 3) // 2
                    pe.wait_ge(s_sdl, k * GBODY + g + 1)
                    if not (isinstance(k, int) and k * GBODY + g + 2 > B):
                        pe.wait_ge(s_hnt, k * GBODY + g + 2)
                    for i in range(NB):
                        for side in range(2):
                            last = nc.tensor.transpose(ps_t[0:16, side * N + i * P:side * N + (i + 1) * P],
                                                       sd[:, i, 4 * side:4 * side + 4], ident[:])
                    last.then_inc(s_lrp, 1)
                if live(-5) and j % 2 == 1:
                    g = (j + 5) // 2
                    r = g % 2
                    pe.wait_ge(s_hnt, k * GBODY + g + 1)
                    freed(pe, s_sdl, k * GBODY + g)
                    for i in range(NB):
                        for c in range(CB):
                            last = nc.tensor.matmul(ps_wh[:, i], hnt[:, r, c, i * P:(i + 1) * P], gw[:, c],
                                                    start=(c == 0), stop=(c == CB - 1))
                    last.then_inc(s_wh, 1)

            scan_slots(pe, HALVES, HBODY, (-6, -5, -3, -1, 2, 3), slot, peeled=2)

            def slot(k, j, live):
                m0 = k * UNITS
                if live(1):
                    m = j - 1
                    q = (m % 2) * 2
                    pe.wait_ge(f_g, m0 + m + 1)
                    freed(pe, f_lo, m0 + m - 1)
                    for c in range(CB):
                        for t in range(UT):
                            last = nc.tensor.transpose(ps[:, q + c, t * P:(t + 1) * P],
                                                       state[:, m % UNITS, t * C + c * P:t * C + (c + 1) * P],
                                                       ident[:])
                    last.then_inc(f_tp, 1)
                if live(3):
                    m = j - 3
                    q, r = 4 + (m % 2) * 2, m % GR
                    pe.wait_ge(f_tc, m0 + m + 1)
                    freed(pe, f_z, m0 + UNITS + m - 1 if not (isinstance(k, int) and m0 + m < 2) else 0)
                    for t in range(HT):
                        for c in range(CB):
                            nc.tensor.matmul(ps[:, q + 1, t * C:(t + 1) * C], g_f[:, r, c, t * P:(t + 1) * P],
                                             w_c[:, c], start=(c == 0), stop=(c == CB - 1))
                    pe.wait_ge(f_lo, m0 + m + 1)
                    for t in range(HT):
                        parts = [(g, w, c) for c in range(CB) for g, w in ((g_hi, w_hi), (g_hi, w_lo), (g_lo, w_hi))]
                        for n, (g, w, c) in enumerate(parts):
                            last = nc.tensor.matmul(ps[:, q, t * C:(t + 1) * C], g[:, r, c, t * P:(t + 1) * P],
                                                    w[:, c], start=(n == 0), stop=(n == len(parts) - 1))
                    last.then_inc(f_mm, 1)

            scan_slots(pe, SLOTS, UNITS, (1, 3), slot)

        @block.scalar
        def _(act):
            def slot(k, j, live):
                if live(2):
                    s, r = j - 2, (j - 2) % 2
                    act.wait_ge(s_te, k * HBODY + s + 1)
                    freed(act, s_o, k * HBODY + s - 1)
                    nc.scalar.activation(ets[:, r].rearrange("p (a h) i n -> p a (h i n)", a=2), ps_et[:],
                                         ACT.Copy).then_inc(s_et, 1)
                if live(0):
                    s, r = j, j % 2
                    act.wait_ge(s_l, k * HBODY + s + 1)
                    act.wait_ge(s_nmx, k * HBODY + s + 1)
                    freed(act, s_rcp, k * HBODY + s - 3)
                    for h in range(HEADS):
                        last = nc.scalar.activation(em[:, s % ER, h], em[:, s % ER, h], ACT.Exp, bias=nmx[:, r, h:h + 1],
                                                    accum_out=rs[:, s % 4, h:h + 1])
                    last.then_inc(s_exp, 1)
                if live(-6) and j % 2 == 0:
                    g = (j + 6) // 2
                    r = g % 2
                    act.wait_ge(s_hnp, k * GBODY + g + 1)
                    freed(act, s_wh, k * GBODY + g - 1)
                    nc.scalar.activation(hnt[:, r], ps_t.rearrange("p (c n) -> p c n", c=CB),
                                         ACT.Copy).then_inc(s_hnt, 1)
                if live(-4) and j % 2 == 0:
                    g = (j + 4) // 2
                    act.wait_ge(s_wh, k * GBODY + g + 1)
                    freed(act, s_o, k * HBODY + 2 * (g - GBODY) + 2)
                    nc.scalar.activation(wh[:, g % GBODY], ps_wh[:, :, 0:C], ACT.Copy).then_inc(s_whc, 1)
                    freed(act, s_lrp, k * GBODY + g)
                    nc.scalar.activation(sd[:, :, 0:8:6].bitcast(F32R),
                                         ps_wh[:, :, C:C + SD].rearrange("p i (a h) -> p i a h", a=2),
                                         ACT.Copy).then_inc(s_sdh, 1)
                if live(-3) and j % 2 == 1:
                    g = (j + 3) // 2
                    r = g % 2
                    act.wait_ge(s_lrp, k * GBODY + g + 1)
                    freed(act, s_e, k * HBODY + 2 * g - 2)
                    freed(act, s_rh, k * GBODY + g - 1)
                    nc.scalar.activation(lr[:, r], ps_t[0:16].rearrange("p (a n) -> p a n", a=2),
                                         ACT.Copy).then_inc(s_lr, 1)
                if live(5) and j % 2 == 1:
                    g = (j - 5) // 2
                    r = g % 2
                    act.wait_ge(s_att, k * HBODY + 2 * g + 2)
                    freed(act, s_x1, k * GBODY + g - 1)
                    nc.scalar.activation(neg[:, r], att[:, g % GBODY], ACT.Exp)
                    nc.scalar.activation(att[:, g % GBODY], att[:, g % GBODY], ACT.Relu).then_inc(s_ex, 1)

            scan_slots(act, HALVES, HBODY, (-6, -4, -3, 0, 2, 5), slot, peeled=2)

            def slot(k, j, live):
                m0 = k * UNITS
                if live(0):
                    m = j
                    act.wait_ge(f_z, m0 + m + 1)
                    freed(act, f_u, m0 + m - TR + 1)
                    nc.scalar.activation(th[:, m % TR], state[:, m % UNITS], ACT.Tanh,
                                         scale=1.0 / GAIN).then_inc(f_t, 1)
                if live(2):
                    m = j - 2
                    q, r = (m % 2) * 2, m % GR
                    act.wait_ge(f_tp, m0 + m + 1)
                    freed(act, f_mm, m0 + m - GR + 1)
                    nc.scalar.activation(g_hi[:, r], ps[:, q:q + 2, 0:HT * P], ACT.Copy)
                    nc.scalar.activation(g_f[:, r], ps[:, q:q + 2, HT * P:UT * P], ACT.Copy).then_inc(f_tc, 1)
                if live(1):
                    m = j - 1
                    act.wait_ge(f_u, m0 + m + 1)
                    nc.scalar.activation(state[:, m % UNITS], state[:, m % UNITS], ACT.Silu,
                                         scale=1.0 / GAIN).then_inc(f_g, 1)

            scan_slots(act, SLOTS, UNITS, (0, 1, 2), slot)

        @block.vector
        def _(dve):
            V = nc.vector
            done = [0]

            def step(ins):
                done[0] += 1
                ins.then_inc(s_set, 1)
                return done[0]

            dve.wait_ge(s_wt, 1)
            step(V.tensor_copy(w_t[:], ps[:, 0].rearrange("p (k c) -> p k c", k=CB)))
            dve.wait_ge(s_set, 1)
            for k in range(CB):
                last = V.tensor_scalar(w_s[:, k], w_t[:, k], lnw[:, k:k + 1], GAIN, ALU.mult, ALU.mult)
            step(last)
            dve.wait_ge(s_id, 11)
            for k in range(CB):
                last = V.tensor_scalar(lnb_wide[:, k], avg[:], 0.0, lnb[:, k:k + 1], ALU.mult, ALU.add)
            step(last)
            dve.wait_ge(s_cm, 1)
            for k in range(CB):
                last = V.tensor_tensor(w_c[:, k], w_s[:, k], ps[:, 1, 0:C], ALU.subtract)
            n = step(last)
            dve.wait_ge(s_set, n)
            n = step(V.tensor_copy(w_hi[:], w_c[:]))
            dve.wait_ge(s_set, n)
            step(V.tensor_tensor(w_lo[:], w_c[:], w_hi[:].bitcast(F32), ALU.subtract))
            dve.wait_ge(s_cv, 1)
            n = step(V.tensor_tensor(c_sum[:], ps[:, 2, 0:C], b_bc[:], ALU.add))
            dve.wait_ge(s_set, n)
            step(V.tensor_scalar(c_bc[:], c_sum[:], GAIN, None, ALU.mult))
            for k in range(CB):
                for side in range(2):
                    n = step(V.tensor_tensor(prod[:], gw[:, k, 0:C].rearrange("p (h d) -> p h d", h=HEADS),
                                             a_bc[:, :, side], ALU.mult))
                    dve.wait_ge(s_set, n)
                    n = step(V.tensor_reduce(gw[:, k, C + HEADS * side:C + HEADS * (side + 1)], prod[:], AX.X,
                                             ALU.add))
                    dve.wait_ge(s_set, n)
            step(V.tensor_scalar(mask[:], adj_i[:], 0.0, MASKED, ALU.is_equal, ALU.mult))
            n = step(V.tensor_scalar(edge[:], adj_i[:], 0.0, None, ALU.not_equal))
            dve.wait_ge(s_set, n)
            step(V.tensor_reduce(has_edge[:], edge[:], AX.X, ALU.max))
            step(V.memset(sd[:], 1.0))
            assert done[0] == SETUP_STEPS

            def slot(k, j, live):
                g0, h0 = k * GBODY, k * HBODY
                if live(0):
                    s, r = j, j % 2
                    dve.wait_ge(s_e, h0 + s + 1)
                    freed(dve, s_te, h0 + s - ER + 1)
                    freed(dve, s_mxl, h0 + s - 1)
                    dve.sem_inc(passed["dve"], 1)
                    for h in range(HEADS):
                        last = V.tensor_tensor_reduce(out=em[:, s % ER, h],
                                                      in0=ps_e[:, h // 2, (h % 2) * N:(h % 2 + 1) * N],
                                                      in1=mask[:, s % NB], scale=1.0, scalar=-3e38,
                                                      op0=ALU.add, op1=ALU.max, accum_out=mx[:, r, h:h + 1])
                    last.then_inc(s_ttr, 1)
                if live(4):
                    s = j - 4
                    i, g4 = s % NB, (s // NB) % GBODY
                    dve.wait_ge(s_o, h0 + s + 1)
                    dve.wait_ge(s_rn, h0 + s + 1)
                    freed(dve, s_x1, g0 + s // NB - GBODY + 1)
                    V.tensor_tensor(att[:, g4, i].rearrange("p (h d) -> p h d", h=HEADS),
                                    ps_o[:, i * C:(i + 1) * C].rearrange("p (h d) -> p h d", h=HEADS),
                                    rnorm[:, s % 4].unsqueeze(2).to_broadcast([P, HEADS, DH]),
                                    ALU.mult).then_inc(s_att, 1)
                if live(0):
                    s, r = j, j % 2
                    e_rows = em[:, s % ER].rearrange("p h n -> p (h n)")
                    dve.wait_ge(s_ttr, h0 + s + 1)
                    V.scalar_tensor_tensor(mxl[:, r], mx[:, r], SLOPE, mx[:, r], ALU.mult,
                                           ALU.max).then_inc(s_mxl, 1)
                    V.scalar_tensor_tensor(e_rows, e_rows, SLOPE, e_rows, ALU.mult, ALU.max).then_inc(s_l, 1)
                    dve.wait_ge(s_mxl, h0 + s + 1)
                    freed(dve, s_exp, h0 + s - 1)
                    V.tensor_scalar(nmx[:, r], mxl[:, r], -1.0, None, ALU.mult).then_inc(s_nmx, 1)
                if live(-3) and j % 2 == 1:
                    g = (j + 3) // 2
                    dve.wait_ge(s_sdh, g0 + g + 1)
                    V.tensor_tensor(sd[:, :, 1:8:6].bitcast(F32R),
                                    ps_wh[:, :, C:C + SD].rearrange("p i (a h) -> p i a h", a=2),
                                    sd[:, :, 0:8:6], ALU.subtract).then_inc(s_sdl, 1)
                if live(1):
                    s = j - 1
                    dve.wait_ge(s_exp, h0 + s + 1)
                    freed(dve, s_rn, h0 + s - 1)
                    V.reciprocal(rcp[:, s % 2], rs[:, s % 4]).then_inc(s_rcp, 1)
                if live(-7) and j % 2 == 1:
                    g = (j + 7) // 2
                    r = g % 2
                    dve.wait_ge(s_grs, g0 + g + 1)
                    freed(dve, s_hnp, g0 + g - 1)
                    for i in range(NB):
                        last = V.tensor_scalar(hn[:, r, i], xin[:, r, i], g_mv[:, r, i, 0:1],
                                               g_rstd[:, r, i:i + 1], ALU.subtract, ALU.mult)
                    last.then_inc(s_hn, 1)
                if live(7) and j % 2 == 1:
                    g = (j - 7) // 2
                    r = g % 2
                    dve.wait_ge(s_ex, g0 + g + 1)
                    V.tensor_scalar(neg[:, r], neg[:, r], 1.0, -1.0, ALU.min, ALU.add).then_inc(s_neg, 1)
                if live(9) and j % 2 == 1:
                    g = (j - 9) // 2
                    r = g % 2
                    dve.wait_ge(s_x1, g0 + g + 1)
                    freed(dve, s_xmv, g0 + g - 1)
                    for i in range(NB):
                        last = V.bn_stats(x_st[:, r, i], xres[:, r, i])
                    last.then_inc(s_xbn, 1)
                if live(-8) and j % 2 == 0:
                    g = (j + 8) // 2
                    r = g % 2
                    dve.wait_ge(s_xin[r], 16 * (2 * k + g // 2 + 1))
                    freed(dve, s_hn, g0 + g - 1)
                    for i in range(NB):
                        last = V.bn_stats(g_st[:, r, i], xin[:, r, i])
                    last.then_inc(s_gbn, 1)
                if live(1):
                    s = j - 1
                    dve.wait_ge(s_rcp, h0 + s + 1)
                    freed(dve, s_att, h0 + s - 3)
                    V.tensor_scalar(rnorm[:, s % 4], rcp[:, s % 2], has_edge[:, s % NB:s % NB + 1], None,
                                    ALU.mult).then_inc(s_rn, 1)
                if live(-8) and j % 2 == 0:
                    g = (j + 8) // 2
                    r = g % 2
                    dve.wait_ge(s_gbn, g0 + g + 1)
                    dve.sem_inc(passed["dve"], 1)
                    for i in range(NB):
                        last = V.bn_aggr(g_mv[:, r, i], g_st[:, r, i])
                    last.then_inc(s_gmv, 1)
                if live(9) and j % 2 == 1:
                    g = (j - 9) // 2
                    r = g % 2
                    dve.wait_ge(s_xbn, g0 + g + 1)
                    freed(dve, s_xve, g0 + g - 1)
                    freed(dve, s_xmc, g0 + g - 1)
                    dve.sem_inc(passed["dve"], 1)
                    for i in range(NB):
                        last = V.bn_aggr(x_mv2[:, r, i], x_st[:, r, i])
                    last.then_inc(s_xmv, 1)

            scan_slots(dve, HALVES, HBODY, (-8, -7, -3, 0, 1, 4, 7, 9), slot, peeled=2)

            def normalise(b, u):
                dve.wait_ge(f_ld[b % 2][u], 16 * (b // 2 + 1))
                for t in range(UT):
                    tile = (b * UNITS + u) * UT + t
                    last = V.tensor_scalar(state[:, u, t * C:(t + 1) * C], x1_sb[:, b % 2, u, t * C:(t + 1) * C],
                                           x_mv[:, tile, 0:1], x_rstd[:, tile:tile + 1], ALU.subtract, ALU.mult)
                last.then_inc(f_z, 1)

            def rest(m0, m):
                q, r = (m % 2) * 2, m % GR
                dve.wait_ge(f_tc, m0 + m + 1)
                freed(dve, f_mm, m0 + m - GR + 1)
                V.tensor_tensor(g_lo[:, r], ps[:, q:q + 2, 0:HT * P], g_hi[:, r].bitcast(F32),
                                ALU.subtract).then_inc(f_lo, 1)

            def stats(m0, m):
                u = m % UNITS
                dve.wait_ge(f_g, m0 + m + 1)
                for t in range(UT):
                    last = V.bn_stats(st[:, u, t], state[:, u, t * C:(t + 1) * C])
                last.then_inc(f_bn, 1)

            def aggregate(m0, m):
                u = m % UNITS
                dve.wait_ge(f_bn, m0 + m + 1)
                dve.sem_inc(passed["dve"], 1)
                for t in range(UT):
                    last = V.bn_aggr(mv[:, u, t], st[:, u, t])
                last.then_inc(f_mv, 1)

            def next_state(m0, m):
                u, q = m % UNITS, 4 + (m % 2) * 2
                dve.wait_ge(f_mm, m0 + m + 1)
                dve.wait_ge(f_rs, m0 + m + 1)
                for t in range(UT):
                    bank, col = divmod((t + HT) % UT, HT)
                    last = V.scalar_tensor_tensor(state[:, u, ((t + HT) % UT) * C:((t + HT) % UT + 1) * C],
                                                  ps[:, q + bank, col * C:(col + 1) * C],
                                                  rstd[:, u, (t + HT) % UT:(t + HT) % UT + 1], c_bc[:],
                                                  ALU.mult, ALU.add)
                return last

            dve.wait_ge(s_xrg, B)
            dve.wait_ge(s_xmc, B)
            for u in range(UNITS):
                normalise(0, u)
            for m in range(3):
                stats(0, m)
                if m < 2:
                    rest(0, m)
                aggregate(0, m)
            for b in range(BATCHES):
                def step_of_all(k, last_step):
                    for u in range(UNITS):
                        z = next_state(k * UNITS, u)
                        if not last_step:
                            z.then_inc(f_z, 1)
                        else:
                            if b + 1 < BATCHES:
                                z.then_inc(f_end, 1)
                                dve.wait_ge(f_end, b * UNITS + u + 1)
                            else:
                                z.then_inc(f_z, 1)
                                dve.wait_ge(f_z, SLOTS + u + 1)
                            V.scalar_tensor_tensor(x1_sb[:, b % 2, u], state[:, u], 1.0 / GAIN,
                                                   x1_sb[:, b % 2, u], ALU.mult, ALU.add).then_inc(f_out, 1)
                            if b + 1 < BATCHES:
                                dve.wait_ge(f_out, b * UNITS + u + 1)
                                normalise(b + 1, u)
                        if not (isinstance(k, int) and k * UNITS + u + 3 >= SLOTS):
                            stats(k * UNITS, u + 3)
                        if not (isinstance(k, int) and k * UNITS + u + 2 >= SLOTS):
                            rest(k * UNITS, u + 2)
                        if not (isinstance(k, int) and k * UNITS + u + 3 >= SLOTS):
                            aggregate(k * UNITS, u + 3)

                first = b * STEPS
                if b == 0:
                    step_of_all(0, False)
                    first = 1
                with dve.Fori(first, (b + 1) * STEPS - 1) as k:
                    step_of_all(k, False)
                step_of_all((b + 1) * STEPS - 1, True)


def kernel(**inputs):
    import concourse.bacc as bacc
    from concourse.bass_utils import run_bass_kernel_spmd

    nc = bacc.Bacc("TRN2", target_bir_lowering=False, num_devices=1)
    names = ["x", "adj", "L0_gnn_W", "L0_gnn_a", "L0_ffn_ln_w", "L0_ffn_ln_b", "L0_ffn_W", "L0_ffn_b"]
    arrays, args = {}, []
    for name in names:
        a = np.ascontiguousarray(inputs[name])
        if name == "x":
            a = a.reshape(ROWS, C)
        arrays["in_" + name] = a
        args.append(nc.dram_tensor("in_" + name, a.shape, mybir.dt.from_np(a.dtype), kind="ExternalInput").ap())
    x1 = nc.dram_tensor("x1_scratch", (ROWS, C), F32, kind="Internal").ap()
    out = nc.dram_tensor("out", (ROWS, C), F32, kind="ExternalOutput").ap()
    build(nc, *args, x1, out)
    r = run_bass_kernel_spmd(nc, [arrays], core_ids=[0])
    return r.results[0]["out"].reshape(B, N, C)
```
